# Optimizing a Trainium2 kernel written in Bass

```python
import numpy as np
import jax
import jax.numpy as jnp

def _softmax(x, axis=-1):
    return jax.nn.softmax(x, axis=axis)

def _gelu(x):
    return jax.nn.gelu(x, approximate=True)

def _silu(x):
    return jax.nn.silu(x)

def _sigmoid(x):
    return jax.nn.sigmoid(x)

def _layernorm(x, axis=-1, eps=1e-05):
    m = jnp.mean(x, axis=axis, keepdims=True)
    v = jnp.var(x, axis=axis, keepdims=True)
    return (x - m) / jnp.sqrt(v + eps)

def _scatter_add(tgt, idx, src, axis=0):
    return tgt.at[idx].add(src)

def _segment_sum(src, seg, n):
    return jax.ops.segment_sum(src, seg, n)
kernel_name = 'mk_gps_d1_gnn_r8_53409f'

def setup_inputs(seed: int=0):
    np.random.seed(seed)
    _w = jnp.asarray

    def _rec_inputs():
        import jax
        import jax.numpy as jnp
        _gk = jax.random.key(seed)
        x = -0.0003713 + 1 * jax.random.normal(jax.random.fold_in(_gk, 1), (6250, 256), jnp.float32)
        src = jax.random.randint(jax.random.fold_in(_gk, 2), (200000,), 0, 6250, jnp.int32)
        dst = jax.random.randint(jax.random.fold_in(_gk, 3), (200000,), 0, 6250, jnp.int32)
        _o = jnp.argsort(dst, stable=True)
        src = src[_o]
        dst = dst[_o]
        return (x, src, dst)
    x, src, dst = _rec_inputs()

    def _L0_gnn_setup():
        import jax, jax.numpy as jnp
        import numpy as np
        N_NODES = 6250
        N_EDGES = 312500
        WIDTH = 256
        LN_EPS = 1e-05

        def gcn_conv(x, edge_index, W, b):
            n = x.shape[0]
            loops = jnp.arange(n, dtype=edge_index.dtype)
            src = jnp.concatenate([edge_index[0], loops])
            dst = jnp.concatenate([edge_index[1], loops])
            deg = jax.ops.segment_sum(jnp.ones_like(dst, dtype=x.dtype), dst, num_segments=n)
            dinv = jnp.where(deg > 0, jax.lax.rsqrt(deg), 0.0)
            norm = dinv[src] * dinv[dst]
            h = x @ W.T
            msgs = norm[:, None] * h[src]
            out = jax.ops.segment_sum(msgs, dst, num_segments=n)
            return out + b

        def layer_norm(x, gamma, beta):
            mu = jnp.mean(x, axis=-1, keepdims=True)
            var = jnp.mean(jnp.square(x - mu), axis=-1, keepdims=True)
            return (x - mu) * jax.lax.rsqrt(var + LN_EPS) * gamma + beta
        key = jax.random.key(seed)
        k1, k2, k3, k4 = jax.random.split(key, 4)
        x = jax.random.normal(k1, (N_NODES, WIDTH), dtype=jnp.float32)
        edge_index = jax.random.randint(k2, (2, N_EDGES), 0, N_NODES, dtype=jnp.int64)
        W = jax.random.normal(k3, (WIDTH, WIDTH), dtype=jnp.float32) / np.sqrt(WIDTH)
        b = jax.random.normal(k4, (WIDTH,), dtype=jnp.float32) * 0.01
        gamma = jnp.ones((WIDTH,), dtype=jnp.float32)
        beta = jnp.zeros((WIDTH,), dtype=jnp.float32)
        return {'x': x, 'edge_index': edge_index, 'W': W, 'b': b, 'gamma': gamma, 'beta': beta}
    _L0_gnn_all = _L0_gnn_setup()
    _L0_gnn_in = {k: v for k, v in _L0_gnn_all.items() if k in ('W', 'b', 'gamma', 'beta')}
    del _L0_gnn_all

    def _L0_mix_setup():
        import jax, jax.numpy as jnp
        import numpy as np
        D_MODEL = 256
        NHEAD = 8
        D_HEAD = D_MODEL // NHEAD
        DIM_FF = 1024
        B, L = (4, 2048)
        LN_EPS = 1e-05

        def _layernorm(x, g, b):
            mu = jnp.mean(x, axis=-1, keepdims=True)
            var = jnp.mean((x - mu) ** 2, axis=-1, keepdims=True)
            return (x - mu) * jax.lax.rsqrt(var + LN_EPS) * g + b

        def _phi(x):
            return jnp.where(x > 0, x + 1.0, jnp.exp(x))
        key = jax.random.key(seed)
        ks = jax.random.split(key, 16)
        s_in = 1.0 / np.sqrt(D_MODEL)
        s_ff = 1.0 / np.sqrt(DIM_FF)
        inp = {'x': jax.random.normal(ks[0], (B, L, D_MODEL), dtype=jnp.float32), 'Wq': jax.random.normal(ks[1], (D_MODEL, D_MODEL), dtype=jnp.float32) * s_in, 'bq': jnp.zeros((D_MODEL,), jnp.float32), 'Wk': jax.random.normal(ks[2], (D_MODEL, D_MODEL), dtype=jnp.float32) * s_in, 'bk': jnp.zeros((D_MODEL,), jnp.float32), 'Wv': jax.random.normal(ks[3], (D_MODEL, D_MODEL), dtype=jnp.float32) * s_in, 'bv': jnp.zeros((D_MODEL,), jnp.float32), 'Wo': jax.random.normal(ks[4], (D_MODEL, D_MODEL), dtype=jnp.float32) * s_in, 'bo': jnp.zeros((D_MODEL,), jnp.float32), 'W1': jax.random.normal(ks[5], (D_MODEL, DIM_FF), dtype=jnp.float32) * s_in, 'b1': jnp.zeros((DIM_FF,), jnp.float32), 'W2': jax.random.normal(ks[6], (DIM_FF, D_MODEL), dtype=jnp.float32) * s_ff, 'b2': jnp.zeros((D_MODEL,), jnp.float32), 'ln1_g': jnp.ones((D_MODEL,), jnp.float32), 'ln1_b': jnp.zeros((D_MODEL,), jnp.float32), 'ln2_g': jnp.ones((D_MODEL,), jnp.float32), 'ln2_b': jnp.zeros((D_MODEL,), jnp.float32)}
        return inp
    _L0_mix_all = _L0_mix_setup()
    _L0_mix_in = {k: v for k, v in _L0_mix_all.items() if k in ('Wq', 'bq', 'Wk', 'bk', 'Wv', 'bv', 'Wo', 'bo', 'W1', 'b1', 'W2', 'b2', 'ln1_g', 'ln1_b', 'ln2_g', 'ln2_b')}
    del _L0_mix_all

    def _L0_ffn_setup():
        import jax, jax.numpy as jnp
        import numpy as np
        TOP_K = 2
        LN_EPS = 1e-05
        key = jax.random.key(seed)
        ks = jax.random.split(key, 8)
        B, S, D, E, H = (16, 1024, 256, 8, 1024)
        x = jax.random.normal(ks[0], (B, S, D), dtype=jnp.float32)
        Wr = jax.random.normal(ks[1], (D, E), dtype=jnp.float32) * 0.1
        br = jnp.zeros((E,), dtype=jnp.float32)
        ln_g = jnp.ones((E, D), dtype=jnp.float32)
        ln_b = jnp.zeros((E, D), dtype=jnp.float32)
        W1 = jax.random.normal(ks[2], (E, D, H), dtype=jnp.float32) * (1.0 / np.sqrt(D))
        b1 = jnp.zeros((E, H), dtype=jnp.float32)
        W2 = jax.random.normal(ks[3], (E, H, D), dtype=jnp.float32) * (1.0 / np.sqrt(H))
        b2 = jnp.zeros((E, D), dtype=jnp.float32)
        return {'x': x, 'Wr': Wr, 'br': br, 'ln_g': ln_g, 'ln_b': ln_b, 'W1': W1, 'b1': b1, 'W2': W2, 'b2': b2}
    _L0_ffn_all = _L0_ffn_setup()
    _L0_ffn_in = {k: v for k, v in _L0_ffn_all.items() if k in ('Wr', 'br', 'ln_g', 'ln_b', 'W1', 'b1', 'W2', 'b2')}
    del _L0_ffn_all
    return {'x': x, 'src': src, 'dst': dst, 'L0_gnn_W': _L0_gnn_in['W'], 'L0_gnn_b': _L0_gnn_in['b'], 'L0_gnn_gamma': _L0_gnn_in['gamma'], 'L0_gnn_beta': _L0_gnn_in['beta'], 'L0_mix_Wq': _L0_mix_in['Wq'], 'L0_mix_bq': _L0_mix_in['bq'], 'L0_mix_Wk': _L0_mix_in['Wk'], 'L0_mix_bk': _L0_mix_in['bk'], 'L0_mix_Wv': _L0_mix_in['Wv'], 'L0_mix_bv': _L0_mix_in['bv'], 'L0_mix_Wo': _L0_mix_in['Wo'], 'L0_mix_bo': _L0_mix_in['bo'], 'L0_mix_W1': _L0_mix_in['W1'], 'L0_mix_b1': _L0_mix_in['b1'], 'L0_mix_W2': _L0_mix_in['W2'], 'L0_mix_b2': _L0_mix_in['b2'], 'L0_mix_ln1_g': _L0_mix_in['ln1_g'], 'L0_mix_ln1_b': _L0_mix_in['ln1_b'], 'L0_mix_ln2_g': _L0_mix_in['ln2_g'], 'L0_mix_ln2_b': _L0_mix_in['ln2_b'], 'L0_ffn_Wr': _L0_ffn_in['Wr'], 'L0_ffn_br': _L0_ffn_in['br'], 'L0_ffn_ln_g': _L0_ffn_in['ln_g'], 'L0_ffn_ln_b': _L0_ffn_in['ln_b'], 'L0_ffn_W1': _L0_ffn_in['W1'], 'L0_ffn_b1': _L0_ffn_in['b1'], 'L0_ffn_W2': _L0_ffn_in['W2'], 'L0_ffn_b2': _L0_ffn_in['b2']}

def reference(x, src, dst, L0_gnn_W, L0_gnn_b, L0_gnn_gamma, L0_gnn_beta, L0_mix_Wq, L0_mix_bq, L0_mix_Wk, L0_mix_bk, L0_mix_Wv, L0_mix_bv, L0_mix_Wo, L0_mix_bo, L0_mix_W1, L0_mix_b1, L0_mix_W2, L0_mix_b2, L0_mix_ln1_g, L0_mix_ln1_b, L0_mix_ln2_g, L0_mix_ln2_b, L0_ffn_Wr, L0_ffn_br, L0_ffn_ln_g, L0_ffn_ln_b, L0_ffn_W1, L0_ffn_b1, L0_ffn_W2, L0_ffn_b2):
    import jax
    import jax.numpy as jnp

    def _L0_gnn_ref(x, edge_index, W, b, gamma, beta):
        import jax, jax.numpy as jnp
        import numpy as np
        N_NODES = 6250
        N_EDGES = 312500
        WIDTH = 256
        LN_EPS = 1e-05

        def gcn_conv(x, edge_index, W, b):
            n = x.shape[0]
            loops = jnp.arange(n, dtype=edge_index.dtype)
            src = jnp.concatenate([edge_index[0], loops])
            dst = jnp.concatenate([edge_index[1], loops])
            deg = jax.ops.segment_sum(jnp.ones_like(dst, dtype=x.dtype), dst, num_segments=n)
            dinv = jnp.where(deg > 0, jax.lax.rsqrt(deg), 0.0)
            norm = dinv[src] * dinv[dst]
            h = x @ W.T
            msgs = norm[:, None] * h[src]
            out = jax.ops.segment_sum(msgs, dst, num_segments=n)
            return out + b

        def layer_norm(x, gamma, beta):
            mu = jnp.mean(x, axis=-1, keepdims=True)
            var = jnp.mean(jnp.square(x - mu), axis=-1, keepdims=True)
            return (x - mu) * jax.lax.rsqrt(var + LN_EPS) * gamma + beta
        h = gcn_conv(x, edge_index, W, b)
        h = layer_norm(h, gamma, beta)
        h = jax.nn.relu(h)
        return h

    def _L0_mix_ref(x, Wq, bq, Wk, bk, Wv, bv, Wo, bo, W1, b1, W2, b2, ln1_g, ln1_b, ln2_g, ln2_b):
        import jax, jax.numpy as jnp
        import numpy as np
        D_MODEL = 256
        NHEAD = 8
        D_HEAD = D_MODEL // NHEAD
        DIM_FF = 1024
        B, L = (4, 2048)
        LN_EPS = 1e-05

        def _layernorm(x, g, b):
            mu = jnp.mean(x, axis=-1, keepdims=True)
            var = jnp.mean((x - mu) ** 2, axis=-1, keepdims=True)
            return (x - mu) * jax.lax.rsqrt(var + LN_EPS) * g + b

        def _phi(x):
            return jnp.where(x > 0, x + 1.0, jnp.exp(x))
        Bq, Lq, _ = x.shape
        q = (x @ Wq + bq).reshape(Bq, Lq, NHEAD, D_HEAD)
        k = (x @ Wk + bk).reshape(Bq, Lq, NHEAD, D_HEAD)
        v = (x @ Wv + bv).reshape(Bq, Lq, NHEAD, D_HEAD)
        q_phi = _phi(q)
        k_phi = _phi(k)
        kv = jnp.einsum('blhd,blhe->bhde', k_phi, v)
        k_sum = k_phi.sum(axis=1)
        z = 1.0 / (jnp.einsum('blhd,bhd->blh', q_phi, k_sum) + 1e-06)
        out = jnp.einsum('blhd,bhde,blh->blhe', q_phi, kv, z)
        out = out.reshape(Bq, Lq, D_MODEL) @ Wo + bo
        x = _layernorm(x + out, ln1_g, ln1_b)
        ff = jax.nn.relu(x @ W1 + b1) @ W2 + b2
        x = _layernorm(x + ff, ln2_g, ln2_b)
        return x

    def _L0_ffn_ref(x, Wr, br, ln_g, ln_b, W1, b1, W2, b2):
        import jax, jax.numpy as jnp
        import numpy as np
        TOP_K = 2
        LN_EPS = 1e-05
        B, S, D = x.shape
        N = B * S
        xt = x.reshape(N, D)
        logits = xt @ Wr + br
        probs = jax.nn.softmax(logits, axis=-1)
        top_p, top_idx = jax.lax.top_k(probs, TOP_K)
        weights = top_p / top_p.sum(axis=-1, keepdims=True)
        mu = xt.mean(axis=-1, keepdims=True)
        var = ((xt - mu) ** 2).mean(axis=-1, keepdims=True)
        xn = (xt - mu) * jax.lax.rsqrt(var + LN_EPS)
        xe = xn[None, :, :] * ln_g[:, None, :] + ln_b[:, None, :]
        h = jax.nn.gelu(jnp.einsum('end,edh->enh', xe, W1) + b1[:, None, :], approximate=False)
        y = jnp.einsum('enh,ehd->end', h, W2) + b2[:, None, :]
        y_tok = jnp.transpose(y, (1, 0, 2))
        sel = jnp.take_along_axis(y_tok, top_idx[:, :, None], axis=1)
        out = (weights[:, :, None] * sel).sum(axis=1)
        return out.reshape(B, S, D)
    edge_index = jnp.stack([src, dst])
    xn = _layernorm(x, axis=-1)
    x = x + _L0_gnn_ref(xn, edge_index, L0_gnn_W, L0_gnn_b, L0_gnn_gamma, L0_gnn_beta) + _L0_mix_ref(xn[None], L0_mix_Wq, L0_mix_bq, L0_mix_Wk, L0_mix_bk, L0_mix_Wv, L0_mix_bv, L0_mix_Wo, L0_mix_bo, L0_mix_W1, L0_mix_b1, L0_mix_W2, L0_mix_b2, L0_mix_ln1_g, L0_mix_ln1_b, L0_mix_ln2_g, L0_mix_ln2_b)[0]
    x = x + _L0_ffn_ref(_layernorm(x, axis=-1)[None], L0_ffn_Wr, L0_ffn_br, L0_ffn_ln_g, L0_ffn_ln_b, L0_ffn_W1, L0_ffn_b1, L0_ffn_W2, L0_ffn_b2)[0]
    return x

_drawn_inputs = setup_inputs


def setup_inputs(seed=0):
    import zlib

    import numpy as np

    out = dict(_drawn_inputs(seed))
    spreads = {'L0_gnn_gamma': (1.0, 0.2),
     'L0_gnn_beta': (0.0, 0.1),
     'L0_mix_bq': (0.0, 0.8),
     'L0_mix_bk': (0.0, 0.8),
     'L0_mix_bv': (0.0, 0.1),
     'L0_mix_bo': (0.0, 0.1),
     'L0_mix_b1': (0.0, 0.1),
     'L0_mix_b2': (0.0, 0.1),
     'L0_mix_ln1_g': (1.0, 0.2),
     'L0_mix_ln1_b': (0.0, 0.1),
     'L0_mix_ln2_g': (1.0, 0.2),
     'L0_mix_ln2_b': (0.0, 0.1),
     'L0_ffn_br': (0.0, 0.1),
     'L0_ffn_ln_g': (1.0, 0.2),
     'L0_ffn_ln_b': (0.0, 0.32),
     'L0_ffn_b1': (0.0, 0.31),
     'L0_ffn_b2': (0.0, 0.1)}
    factors = {'L0_mix_Wq': 6.703, 'L0_mix_Wk': 5.466, 'L0_mix_Wv': 4.318}
    for name, (base, spread) in spreads.items():
        noise = np.random.default_rng([zlib.crc32(name.encode()), seed]).standard_normal(out[name].shape)
        drawn = base * np.exp(spread * noise) if base else spread * noise
        out[name] = jnp.asarray(drawn.astype(out[name].dtype))
    for name, factor in factors.items():
        out[name] = (out[name] * factor).astype(out[name].dtype)
    return out
```

```python
from contextlib import ExitStack

import concourse.bass as bass
from concourse import mybir

F32 = mybir.dt.float32
F16 = mybir.dt.float16
I32 = mybir.dt.int32
ALU = mybir.AluOpType
ACT = mybir.ActivationFunctionType
AX = mybir.AxisListType

NODES = 6250
EDGES = 200000
D = 256
KD = D // 128
R = 125
TILES = NODES // R
PAIRS = TILES // 2
HEADS = 8
DH = D // HEADS
FF = 1024
FC = FF // 128
EXP = 8
GT = 16
GE = GT * R
GROUPS = EDGES // GE
SLOTS = 4
ROUNDS = GROUPS // SLOTS
ET = 256
ETILES = (2 * NODES + EXP * (ET - 1)) // ET
CAP = ETILES * ET
EPS = 1e-5
SCALE = 2048.0
ROUND = 12582912.0
LOWEST = -3.0e38
assert ROUNDS == PAIRS and GROUPS * GE == EDGES and ETILES % 2 == 0


def gps_layer(nc, a, out):
    ctx = ExitStack()
    with ctx:
        def sb(name, shape, dt=F32):
            return ctx.enter_context(nc.sbuf_tensor(name, shape, dt))

        def sem(name):
            return ctx.enter_context(nc.semaphore(name))

        def scratch(name, shape, dt=F32):
            return nc.dram_tensor(name, shape, dt, kind="Internal").ap()

        def pairs(ap):
            return ap.rearrange("(i u p) d -> i p u d", u=2, p=R)

        xn_d = scratch("xn_d", (NODES, D))
        msg_d = scratch("msg_d", (NODES, 2 * D), F16)
        mix_d = scratch("mix_d", (NODES + 2 * R, D))
        x2_d = scratch("x2_d", (NODES, D))
        slot_d = scratch("slot_d", (CAP + ET, D))
        y_d = scratch("y_d", (CAP, D))

        sums = ctx.enter_context(nc.psum_tensor("sums", [128, 1024], F32))
        bank = [sums[:, 0:512], sums[:, 512:1024]]
        bank += [ctx.enter_context(nc.psum_tensor(f"bank{k}", [128, 512], F32)) for k in range(2, 8)]

        ident = sb("ident", [128, 128])
        ones = sb("ones", [128, 128])
        before = sb("before", [R, R])
        eps_col = sb("eps_col", [128, 1])
        iota_r = sb("iota_r", [R, R, GT], F16)
        iota_t = sb("iota_t", [R, TILES, GT], F16)
        tile_off = sb("tile_off", [R, TILES])
        headmask = sb("headmask", [128, 4])
        degree = sb("degree", [R, TILES])
        dinv = sb("dinv", [R, TILES])
        dinv_up = sb("dinv_up", [R, TILES])
        dinv_down = sb("dinv_down", [R, TILES])
        dst_g = sb("dst_g", [R, GROUPS, GT])
        span = sb("span", [1, 2 * GROUPS + 1], I32)
        kvbd = sb("kvbd", [128, 2, 128 + 4])
        acc = sb("acc", [R, TILES * D])
        logits = sb("logits", [R, TILES, EXP])
        weights = sb("weights", [R, TILES, 2])
        place = sb("place", [R, TILES, 2], I32)
        expert_of = sb("expert_of", [1, ETILES + 1], I32)
        rank = sb("rank", [R, EXP])
        tile_no = sb("tile_no", [1, ETILES + 1])
        row_bias = {n: sb("row_" + n, [128, D]) for n in
                    ("bo", "b2", "ln1_g", "ln1_b", "ln2_g", "ln2_b", "gnn_b", "gnn_gamma", "gnn_beta")}
        row_kv = sb("row_kv", [128, 2 * D])
        row_br = sb("row_br", [128, EXP])
        col_bq = sb("col_bq", [128, KD])
        col_b1 = sb("col_b1", [128, FC])
        w_q = sb("w_q", [128, KD, D])
        w_o = sb("w_o", [128, KD, D])
        w_kv = sb("w_kv", [128, KD, 2 * D])
        w_gt = sb("w_gt", [128, KD, D])
        w_r = sb("w_r", [128, KD, EXP])

        passed_sp, passed_pool, passed_pe = sem("passed_sp"), sem("passed_pool"), sem("passed_pe")

        loaded = sem("loaded")
        made_0 = sem("made_0")
        wt_there = sem("wt_there")
        with ExitStack() as s:
            w_gn = s.enter_context(nc.sbuf_tensor("w_gn", [128, KD, D], F32))
            zero = s.enter_context(nc.sbuf_tensor("zero", [128, 2 * D], F32))
            zero_made = sem("zero_made")
            zeroed = sem("zeroed")
            loads = 17
            with nc.Block() as block:
                @block.sync
                def _(sp):
                    def parts(w):
                        return w.rearrange("(k p) n -> p k n", p=128)
                    sp.dma_start(w_gn[:, :, :], parts(a["gnn_W"])).then_inc(loaded, 16)
                    sp.dma_start(w_q[:, :, :], parts(a["Wq"])).then_inc(loaded, 16)
                    sp.dma_start(w_kv[:, :, 0:D], parts(a["Wk"])).then_inc(loaded, 16)
                    sp.dma_start(w_kv[:, :, D:2 * D], parts(a["Wv"])).then_inc(loaded, 16)
                    sp.dma_start(w_o[:, :, :], parts(a["Wo"])).then_inc(loaded, 16)
                    sp.dma_start(w_r[:, :, :], parts(a["Wr"])).then_inc(loaded, 16)
                    for n, t in row_bias.items():
                        sp.dma_start(t[:, :], a[n].partition_broadcast(128)).then_inc(loaded, 16)
                    sp.dma_start(row_kv[:, 0:D], a["bk"].partition_broadcast(128)).then_inc(loaded, 16)
                    sp.dma_start(row_kv[:, D:2 * D], a["bv"].partition_broadcast(128)).then_inc(loaded, 16)
                    sp.wait_ge(zero_made, 1)
                    sp.dma_start(slot_d.rearrange("(n p k) d -> p n (k d)", p=128, k=2),
                                 zero[:, :].unsqueeze(1).broadcast_to([128, ETILES + 1, 2 * D])).then_inc(zeroed, 16)
                    sp.wait_ge(loaded, 16 * loads)
                    sp.wait_ge(zeroed, 16)

                more = sem("more")

                @block.scalar
                def _(act):
                    act.dma_start(row_br[:, :], a["br"].partition_broadcast(128)).then_inc(more, 16)
                    act.dma_start(col_bq[:, :], a["bq"].rearrange("(k p) -> p k", p=128),
                                  allow_slow_non_contiguous=True).then_inc(more, 16)
                    act.dma_start(col_b1[:, :], a["b1"].rearrange("(k p) -> p k", p=128),
                                  allow_slow_non_contiguous=True).then_inc(more, 16)
                    act.wait_ge(more, 48)

                @block.vector
                def _(dve):
                    dve.memset(zero[:, :], 0.0).then_inc(zero_made, 1)
                    dve.memset(headmask[:, :], 0.0)
                    dve.memset(degree[:, :], 1.0)
                    dve.drain()
                    for h in range(4):
                        dve.memset(headmask[DH * h:DH * (h + 1), h:h + 1], 1.0)
                    dve.wait_ge(wt_there, 1)
                    for k in range(KD):
                        dve.tensor_copy(w_gt[:, k, :], bank[k][:, 0:D])

                @block.gpsimd
                def _(pool):
                    pool.memset(ident[:, :], 0.0)
                    pool.memset(ones[:, :], 1.0)
                    pool.memset(eps_col[:, :], EPS)
                    pool.memset(before[:, :], 1.0)
                    pool.drain()
                    pool.affine_select(out=ident[:, :], in_=ident[:, :], compare_op=ALU.not_equal, fill=1.0,
                                       base=0, pattern=[[-1, 128]], channel_multiplier=1).then_inc(made_0, 1)
                    pool.affine_select(out=before[:, :], in_=before[:, :], compare_op=ALU.is_gt, fill=0.0,
                                       base=0, pattern=[[1, R]], channel_multiplier=-1)
                    pool.iota(iota_r[:, :, :], [[1, R], [0, GT]], base=0, channel_multiplier=0,
                              allow_small_or_imprecise_dtypes=True)
                    pool.iota(iota_t[:, :, :], [[1, TILES], [0, GT]], base=0, channel_multiplier=0,
                              allow_small_or_imprecise_dtypes=True)
                    pool.iota(rank[:, :], [[-1, EXP]], base=EXP, channel_multiplier=0,
                              allow_small_or_imprecise_dtypes=True)
                    pool.iota(tile_no[:, :], [[1, ETILES + 1]], base=0, channel_multiplier=0,
                              allow_small_or_imprecise_dtypes=True)
                    pool.iota(tile_off[:, :], [[R, TILES]], base=0, channel_multiplier=0,
                              allow_small_or_imprecise_dtypes=True)

                @block.tensor
                def _(pe):
                    pe.wait_ge(made_0, 1)
                    pe.wait_ge(loaded, 16 * loads)
                    for k in range(KD):
                        for m in range(KD):
                            last = pe.transpose(bank[k][:, m * 128:(m + 1) * 128],
                                                w_gn[:, m, k * 128:(k + 1) * 128], ident[:, :])
                    last.then_inc(wt_there, 1)


        def ln_stats(dve, rows, stats, mv, var_made):
            for u in range(2):
                dve.bn_stats(stats[:, u, :], rows[:, u, :])
            dve.drain()
            for u in range(2):
                last = dve.bn_aggr(mv[:, u, :], stats[:, u, :])
            last.then_inc(var_made, 1)

        def ln_root(act, mv, std, root_made):
            act.activation(std[:, :], mv[:, :, 1], ACT.Sqrt, bias=eps_col[0:R, :]).then_inc(root_made, 1)

        def ln_scale(dve, out_rows, rows, mv, std, rstd):
            dve.reciprocal(rstd[:, :], std[:, :])
            dve.drain()
            for u in range(2):
                last = dve.tensor_scalar(out_rows[:, u, :], rows[:, u, :], mv[:, u, 0:1], rstd[:, u:u + 1],
                                         ALU.subtract, ALU.mult)
            return last

        def both(row):
            return row[0:R, :].unsqueeze(1).broadcast_to([R, 2, D])

        with ExitStack() as s:
            def tb(name, shape, dt=F32):
                return s.enter_context(nc.sbuf_tensor(name, shape, dt))

            x_in = tb("x_in", [R, 2, 2, D])
            xn = tb("xn", [R, 2, D])
            stats = tb("n_stats", [R, 2, 6])
            mv = tb("n_mv", [R, 2, 2])
            std = tb("n_std", [R, 2])
            rstd = tb("n_rstd", [R, 2])
            xnT = tb("xnT", [128, KD, 2 * R])
            k_b = tb("k_b", [R, 2, D])
            k_e = tb("k_e", [R, 2, D])
            k_r = tb("k_r", [R, 2, D])
            k_phi = tb("k_phi", [R, 2, D])
            v_aug = tb("v_aug", [R, 2, 2, 129])
            kv_sum = tb("kv_sum", [128, 2, 129])
            lo = tb("lo", [R, EDGES // R], F16)
            hi = tb("hi", [R, EDGES // R], F16)
            is_lo = tb("is_lo", [R, 2, R, GT], F16)
            is_hi = tb("is_hi", [R, 2, TILES, GT], F16)
            d_i = tb("d_i", [R, EDGES // R], I32)
            d_f = tb("d_f", [R, EDGES // R])
            d_h = tb("d_h", [R, EDGES // R])
            g_i = tb("g_i", [GROUPS, GE], I32)
            ends = tb("ends", [GROUPS, 2])
            ends_t = tb("ends_t", [GROUPS, 2])
            row = tb("row", [1, 5, GROUPS])

            n_dst, n_dstg = sem("n_dst"), sem("n_dstg")
            n_x, n_x_free, n_var, n_root, n_xn = sem("n_x"), sem("n_x_free"), sem("n_var"), sem("n_root"), sem("n_xn")
            n_stored, n_xT_ps, n_xT, n_kv_ps, n_kb = (sem("n_stored"), sem("n_xT_ps"), sem("n_xT"),
                                                      sem("n_kv_ps"), sem("n_kb"))
            n_ke, n_phi, n_sum_ps, n_is, n_deg = sem("n_ke"), sem("n_phi"), sem("n_sum_ps"), sem("n_is"), sem("n_deg")
            n_deg_read = sem("n_deg_read")
            n_ends, n_ends_ps = sem("n_ends"), sem("n_ends_ps")
            x_v, xn_v = pairs(a["x"]), pairs(xn_d)
            CH = 4

            with nc.Block() as block:
                @block.sync
                def _(sp):
                    sp.dma_start(d_i[:, :], a["dst"].rearrange("(p j) -> p j", p=R)).then_inc(n_dst, 16)
                    sp.dma_start(g_i[:, :], a["dst"].rearrange("(g j) -> g j", g=GROUPS)).then_inc(n_dstg, 16)
                    with sp.Fori(0, PAIRS) as i:
                        sp.wait_ge(n_x, i * 16)
                        sp.sem_inc(passed_sp, 1)
                        sp.wait_ge(n_x_free, i + 1)
                        sp.sem_inc(passed_sp, 1)
                        sp.dma_start(x_in[:, bass.ds(i % 2, 1), :, :].squeeze(1), x_v[i]).then_inc(n_x, 16)
                    sp.wait_ge(n_x, 16 * PAIRS)

                @block.gpsimd
                def _(pool):
                    with pool.Fori(0, PAIRS) as i:
                        pool.wait_ge(n_stored, i * 16)
                        pool.sem_inc(passed_pool, 1)
                        pool.wait_ge(n_xn, i + 1)
                        pool.sem_inc(passed_pool, 1)
                        pool.dma_start(xn_v[i], xn[:, :, :]).then_inc(n_stored, 16)
                    pool.wait_ge(n_stored, 16 * PAIRS)

                @block.vector
                def _(dve):
                    dve.memset(kv_sum[:, :, :], 0.0)
                    dve.memset(v_aug[:, :, :, :], 1.0).then_inc(n_x_free, 2)
                    dve.wait_ge(n_dst, 16)
                    dve.tensor_copy(d_f[:, :], d_i[:, :])
                    dve.drain()
                    dve.tensor_scalar(d_h[:, :], d_f[:, :], -float(R // 2), 1.0 / R, ALU.add, ALU.mult)
                    dve.drain()
                    dve.tensor_scalar(d_h[:, :], d_h[:, :], ROUND, -ROUND, ALU.add, ALU.add)
                    dve.drain()
                    dve.tensor_copy(hi[:, :], d_h[:, :])
                    dve.scalar_tensor_tensor(out=lo[:, :], in0=d_h[:, :], scalar=-float(R), in1=d_f[:, :],
                                             op0=ALU.mult, op1=ALU.add)
                    dve.wait_ge(n_dstg, 16)
                    dve.tensor_reduce(ends[:, 0:1], g_i[:, :], AX.X, ALU.min)
                    dve.tensor_reduce(ends[:, 1:2], g_i[:, :], AX.X, ALU.max)
                    dve.drain()
                    dve.tensor_scalar(ends_t[:, :], ends[:, :], -float(R // 2), 1.0 / R, ALU.add, ALU.mult)
                    dve.drain()
                    dve.tensor_scalar(ends_t[:, :], ends_t[:, :], ROUND, -ROUND, ALU.add, ALU.add).then_inc(n_ends, 1)
                    dve.wait_ge(n_ends_ps, 1)
                    dve.tensor_copy(row[:, 0, :], bank[7][0:1, 0:GROUPS])
                    dve.tensor_copy(row[:, 1, :], bank[7][0:1, 128:128 + GROUPS])
                    dve.drain()
                    dve.scalar_tensor_tensor(out=row[:, 2, :], in0=row[:, 1, :], scalar=1.0, in1=row[:, 0, :],
                                             op0=ALU.add, op1=ALU.subtract)
                    dve.drain()
                    dve.tensor_tensor_scan(row[:, 3, :], ones[0:1, 0:GROUPS], row[:, 2, :], 0.0, ALU.mult, ALU.add)
                    dve.drain()
                    dve.tensor_tensor(row[:, 4, :], row[:, 3, :], row[:, 2, :], ALU.subtract)
                    dve.drain()
                    dve.tensor_copy(span[:, 0:GROUPS], row[:, 4, :])
                    dve.tensor_copy(span[:, GROUPS:GROUPS + 1], row[:, 3, GROUPS - 1:GROUPS])
                    dve.tensor_tensor(span[:, GROUPS + 1:2 * GROUPS + 1], row[:, 0, :], row[:, 4, :], ALU.subtract)

                    def digits(i, c):
                        col = (i * CH + c) * GT
                        dve.wait_ge(n_deg, i * CH + c)
                        dve.tensor_tensor(is_lo[:, c % 2, :, :], iota_r[:, :, :],
                                          lo[:, bass.ds(col, GT)].unsqueeze(1).broadcast_to([R, R, GT]),
                                          ALU.is_equal)
                        dve.tensor_tensor(is_hi[:, c % 2, :, :], iota_t[:, :, :],
                                          hi[:, bass.ds(col, GT)].unsqueeze(1).broadcast_to([R, TILES, GT]),
                                          ALU.is_equal).then_inc(n_is, 1)

                    with dve.Fori(0, PAIRS) as i:
                        x_row = x_in[:, bass.ds(i % 2, 1), :, :].squeeze(1)
                        dve.wait_ge(n_x, i * 16 + 16)
                        ln_stats(dve, x_row, stats, mv, n_var)
                        digits(i, 0)
                        dve.wait_ge(n_root, i + 1)
                        dve.wait_ge(n_stored, i * 16)
                        ln_scale(dve, xn, x_row, mv, std, rstd).then_inc(n_xn, 1)
                        dve.drain()
                        dve.sem_inc(n_x_free, 1)
                        digits(i, 1)
                        dve.wait_ge(n_kv_ps, i + 1)
                        for u in range(2):
                            dve.tensor_tensor(k_b[:, u, :], bank[1 + u][0:R, 0:D], row_kv[0:R, 0:D], ALU.add)
                        dve.drain().then_inc(n_kb, 1)
                        for u in range(2):
                            dve.tensor_tensor(v_aug[:, u, :, 0:128],
                                              bank[1 + u][0:R, D:2 * D].rearrange("p (h d) -> p h d", h=2),
                                              row_kv[0:R, D:2 * D].rearrange("p (h d) -> p h d", h=2), ALU.add)
                        dve.tensor_scalar(k_r[:, :, :], k_b[:, :, :], 0.0, None, ALU.max)
                        digits(i, 2)
                        dve.drain()
                        dve.wait_ge(n_ke, i + 1)
                        dve.scalar_tensor_tensor(out=k_phi[:, :, :], in0=k_e[:, :, :], scalar=1.0,
                                                 in1=k_r[:, :, :], op0=ALU.min, op1=ALU.add)
                        dve.drain().then_inc(n_phi, 1)
                        digits(i, 3)
                        dve.wait_ge(n_sum_ps, i + 1)
                        dve.tensor_tensor(kv_sum[:, :, :], bank[3][:, 0:258].rearrange("p (h d) -> p h d", h=2),
                                          kv_sum[:, :, :], ALU.add)
                        dve.drain()
                        dve.wait_ge(n_deg, i * CH + CH)
                        dve.tensor_tensor(degree[:, :], bank[4][0:R, 0:TILES], degree[:, :], ALU.add) \
                            .then_inc(n_deg_read, 1)
                        dve.drain()
                    for h in range(2):
                        dve.tensor_tensor(kvbd[:, h, 0:128].rearrange("p (a d) -> p a d", a=4),
                                          kv_sum[:, h, 0:128].rearrange("p (a d) -> p a d", a=4),
                                          headmask[:, :].unsqueeze(2).broadcast_to([128, 4, DH]), ALU.mult)
                        dve.tensor_scalar(kvbd[:, h, 128:132], headmask[:, :], kv_sum[:, h, 128:129], None, ALU.mult)

                @block.scalar
                def _(act):
                    with act.Fori(0, PAIRS) as i:
                        act.wait_ge(n_var, i + 1)
                        ln_root(act, mv, std, n_root)
                        act.wait_ge(n_xT_ps, i + 1)
                        act.copy(xnT[:, :, :], bank[0][:, 0:4 * R].rearrange("p (k n) -> p k n", k=KD)) \
                            .then_inc(n_xT, 1)
                        act.wait_ge(n_kb, i + 1)
                        act.activation(k_e[:, :, :], k_b[:, :, :], ACT.Exp).then_inc(n_ke, 1)

                @block.tensor
                def _(pe):
                    def counts(i, c):
                        pe.wait_ge(n_is, i * CH + c + 1)
                        if c == 0:
                            pe.wait_ge(n_deg_read, i)
                        for j in range(GT):
                            last = pe.matmul(bank[4][0:R, 0:TILES], is_lo[:, c % 2, :, j], is_hi[:, c % 2, :, j],
                                             start=(c == 0 and j == 0), stop=(c == CH - 1 and j == GT - 1))
                        last.then_inc(n_deg, 1)

                    pe.wait_ge(n_ends, 1)
                    pe.transpose(bank[7][0:1, 0:GROUPS], ends_t[:, 0:1], ident[0:GROUPS, 0:GROUPS])
                    pe.transpose(bank[7][0:1, 128:128 + GROUPS], ends_t[:, 1:2], ident[0:GROUPS, 0:GROUPS]) \
                        .then_inc(n_ends_ps, 1)
                    with pe.Fori(0, PAIRS) as i:
                        counts(i, 0)
                        pe.wait_ge(n_xn, i + 1)
                        for k in range(KD):
                            for u in range(2):
                                last = pe.transpose(bank[0][:, (2 * k + u) * R:(2 * k + u + 1) * R],
                                                    xn[:, u, k * 128:(k + 1) * 128],
                                                    ident[0:R, 0:R])
                        last.then_inc(n_xT_ps, 1)
                        pe.wait_ge(n_xT, i + 1)
                        for u in range(2):
                            for k in range(KD):
                                last = pe.matmul(bank[1 + u][0:R, :], xnT[:, k, u * R:(u + 1) * R], w_kv[:, k, :],
                                                 start=(k == 0), stop=(k == KD - 1))
                        last.then_inc(n_kv_ps, 1)
                        counts(i, 1)
                        counts(i, 2)
                        pe.wait_ge(n_phi, i + 1)
                        for h in range(2):
                            for u in range(2):
                                last = pe.matmul(bank[3][:, h * 129:(h + 1) * 129],
                                                 k_phi[:, u, h * 128:(h + 1) * 128], v_aug[:, u, h, :],
                                                 start=(u == 0), stop=(u == 1))
                        last.then_inc(n_sum_ps, 1)
                        counts(i, 3)

        inv_there, root_there, dst_there = sem("inv_there"), sem("root_there"), sem("dst_there")
        with ExitStack() as s:
            inv = s.enter_context(nc.sbuf_tensor("inv", [R, TILES], F32))
            dst_i = s.enter_context(nc.sbuf_tensor("dst_i", [R, GROUPS, GT], I32))
            with nc.Block() as block:
                @block.sync
                def _(sp):
                    sp.dma_start(dst_i[:, :, :], a["dst"].rearrange("(g p j) -> p g j", p=R, j=GT)) \
                        .then_inc(dst_there, 16)

                @block.vector
                def _(dve):
                    dve.reciprocal(inv[:, :], degree[:, :]).then_inc(inv_there, 1)
                    dve.wait_ge(root_there, 1)
                    dve.tensor_scalar(dinv_up[:, :], dinv[:, :], SCALE, None, ALU.mult)
                    dve.tensor_scalar(dinv_down[:, :], dinv[:, :], 1.0 / SCALE, None, ALU.mult)
                    dve.wait_ge(dst_there, 16)
                    dve.tensor_copy(dst_g[:, :, :], dst_i[:, :, :])

                @block.scalar
                def _(act):
                    act.wait_ge(inv_there, 1)
                    act.activation(dinv[:, :], inv[:, :], ACT.Sqrt).then_inc(root_there, 1)

        with ExitStack() as s:
            xn_m = s.enter_context(nc.sbuf_tensor("xn_m", [R, 2, 2, D], F32))
            msg = s.enter_context(nc.sbuf_tensor("msg", [R, 2, 2, 2 * D], F16))
            m_in, m_free, m_made, m_out = sem("m_in"), sem("m_free"), sem("m_made"), sem("m_out")
            xn_v, msg_v = pairs(xn_d), pairs(msg_d)
            with nc.Block() as block:
                @block.sync
                def _(sp):
                    with sp.Fori(0, PAIRS) as i:
                        sp.wait_ge(m_in, i * 16)
                        sp.sem_inc(passed_sp, 1)
                        sp.wait_ge(m_free, i + 1)
                        sp.sem_inc(passed_sp, 1)
                        sp.dma_start(xn_m[:, bass.ds(i % 2, 1), :, :].squeeze(1), xn_v[i]).then_inc(m_in, 16)
                    sp.wait_ge(m_in, 16 * PAIRS)

                @block.gpsimd
                def _(pool):
                    with pool.Fori(0, PAIRS) as i:
                        pool.wait_ge(m_out, i * 16)
                        pool.sem_inc(passed_pool, 1)
                        pool.wait_ge(m_made, i + 1)
                        pool.sem_inc(passed_pool, 1)
                        pool.dma_start(msg_v[i], msg[:, bass.ds(i % 2, 1), :, :].squeeze(1)).then_inc(m_out, 16)
                    pool.wait_ge(m_out, 16 * PAIRS)

                @block.vector
                def _(dve):
                    dve.sem_inc(m_free, 2)
                    with dve.Fori(0, PAIRS) as i:
                        half = msg[:, bass.ds(i % 2, 1), :, :].squeeze(1)
                        own = acc[:, bass.ds(i * (2 * D), 2 * D)].rearrange("p (u d) -> p u d", u=2)
                        dve.wait_ge(m_in, i * 16 + 16)
                        for u in range(2):
                            dve.tensor_scalar(acc[:, bass.ds((i * 2 + u) * D, D)],
                                              xn_m[:, bass.ds(i % 2, 1), u, :].squeeze(1),
                                              dinv_up[:, bass.ds(i * 2 + u, 1)], None, ALU.mult)
                        dve.drain().then_inc(m_free, 1)
                        dve.wait_ge(m_out, i * 16)
                        dve.tensor_copy(half[:, :, 0:D], own)
                        dve.drain()
                        dve.tensor_tensor(half[:, :, D:2 * D], own, half[:, :, 0:D], ALU.subtract) \
                            .then_inc(m_made, 1)

        with ExitStack() as s:
            def tb(name, shape, dt=F32):
                return s.enter_context(nc.sbuf_tensor(name, shape, dt))

            ring = tb("ring", [R, SLOTS, GT, 2 * D], F16)
            idx = tb("idx", [R, SLOTS, GT], I32)
            one_hot = tb("one_hot", [R, 2, R, GT], F16)
            rel = tb("rel", [R, 2, GT], F16)
            w_1 = tb("w_1", [128, KD, FF])
            w_2 = tb("w_2", [128, FC, D])
            xn_p = tb("xn_p", [R, 2, D])
            xT = tb("xT", [128, KD, 2 * R])
            q_e = tb("q_e", [128, KD, 2 * R])
            q_r = tb("q_r", [128, KD, 2 * R])
            q_phi = tb("q_phi", [128, KD, 2 * R])
            den = tb("den", [R, 2, 2, 4])
            zed = tb("zed", [R, 2, 2, 4])
            att = tb("att", [R, 2, D])
            attT = tb("attT", [128, KD, 2 * R])
            res = tb("res", [R, 2, D])
            x1 = tb("x1", [R, 2, D])
            ff = tb("ff", [128, FC, 2 * R])
            mix = tb("mix", [R, 2, D])
            stats = tb("p_stats", [R, 2, 6])
            mv = tb("p_mv", [R, 2, 2])
            std = tb("p_std", [R, 2])
            rstd = tb("p_rstd", [R, 2])

            gathered = [sem(f"gathered{q}") for q in range(SLOTS)]
            idx_there = [sem(f"idx_there{q}") for q in range(SLOTS)]
            ring_read = [sem(f"ring_read{q}") for q in range(SLOTS)]
            w1_there, w2_there = sem("w1_there"), sem("w2_there")
            hot_made, hot_used, sums_made, sums_kept = (sem("hot_made"), sem("hot_used"), sem("sums_made"),
                                                        sem("sums_kept"))
            p_x, p_x_free, p_xT_ps, p_xT, p_q_ps, p_qe, p_q = (sem("p_" + n) for n in
                                                              ("x", "x_free", "xT_ps", "xT", "q_ps", "qe", "q"))
            p_num, p_att, p_attT_ps, p_attT, p_proj = (sem("p_" + n) for n in
                                                       ("num", "att", "attT_ps", "attT", "proj"))
            p_var, p_root, p_x1, p_x1T_ps, p_x1T, p_f1, p_ff, p_f2 = (sem("p_" + n) for n in (
                "var", "root", "x1", "x1T_ps", "x1T", "f1", "ff", "f2"))
            p_mix, p_stored = sem("p_mix"), sem("p_stored")
            xn_v, mix_v = pairs(xn_d), pairs(mix_d)
            src_v = a["src"].rearrange("(g p j) -> g p j", p=R, j=GT)

            def steps(eng, g):
                first = eng.value_load(span[0:1, bass.ds(g, 1)], min_val=0, max_val=GROUPS * TILES)
                last = eng.value_load(span[0:1, bass.ds(g + 1, 1)], min_val=0, max_val=GROUPS * TILES)
                shift = eng.value_load(span[0:1, bass.ds(g + (GROUPS + 1), 1)], min_val=-GROUPS * TILES,
                                       max_val=TILES)
                return first, last, shift

            def tile_of(eng, n, shift):
                return nc.s_assert_within(eng.snap(n + shift), 0, TILES - 1,
                                      skip_runtime_bounds_check_because="span holds the steps by group")

            with nc.Block() as block:
                @block.sync
                def _(sp):
                    sp.dma_start(w_1[:, :, :], a["W1"].rearrange("(k p) n -> p k n", p=128)).then_inc(w1_there, 16)
                    sp.dma_start(w_2[:, :, :], a["W2"].rearrange("(k p) n -> p k n", p=128)).then_inc(w2_there, 16)
                    with sp.Fori(0, ROUNDS) as i:
                        for q in range(SLOTS):
                            sp.wait_ge(gathered[q], i * (16 * GT))
                            sp.sem_inc(passed_sp, 1)
                            sp.dma_start(idx[:, q, :], src_v[i * SLOTS + q]).then_inc(idx_there[q], 16)
                            if q == 0:
                                sp.wait_ge(p_x_free, i + 1)
                                sp.sem_inc(passed_sp, 1)
                                sp.dma_start(xn_p[:, :, :], xn_v[i]).then_inc(p_x, 16)
                            if q == 2:
                                sp.wait_ge(p_mix, i + 1)
                                sp.sem_inc(passed_sp, 1)
                                sp.dma_start(mix_v[i], mix[:, :, :]).then_inc(p_stored, 16)
                    sp.wait_ge(p_mix, PAIRS + 1)
                    sp.dma_start(mix_v[PAIRS], mix[:, :, :]).then_inc(p_stored, 16)
                    sp.wait_ge(p_stored, 16 * (PAIRS + 1))

                @block.gpsimd
                def _(pool):
                    with pool.Fori(0, ROUNDS) as i:
                        for q in range(SLOTS):
                            pool.wait_ge(idx_there[q], i * 16 + 16)
                            pool.sem_inc(passed_pool, 1)
                            pool.wait_ge(ring_read[q], i)
                            pool.sem_inc(passed_pool, 1)
                            for j in range(GT):
                                pool.indirect_dma_start(
                                    ring[:, q, j, :], None, msg_d,
                                    bass.IndirectOffsetOnAxis(idx[:, q, j:j + 1], 0)).then_inc(gathered[q], 16)

                @block.vector
                def _(dve):
                    def one_hots(i, q):
                        g = i * SLOTS + q
                        first, last, shift = steps(dve, g)
                        with dve.Fori(first, last) as n:
                            tile = tile_of(dve, n, shift)
                            dve.tensor_scalar(rel[:, bass.ds(n % 2, 1), :].squeeze(1),
                                              dst_g[:, bass.ds(g, 1), :].squeeze(1),
                                              tile_off[:, bass.ds(tile, 1)], None, ALU.subtract)
                            dve.drain()
                            dve.wait_ge(hot_used, n)
                            dve.tensor_tensor(
                                one_hot[:, bass.ds(n % 2, 1), :, :].squeeze(1), iota_r[:, :, :],
                                rel[:, bass.ds(n % 2, 1), :].broadcast_to([R, R, GT]),
                                ALU.is_equal).then_inc(hot_made, 1)

                    dve.memset(mix[:, :, :], 0.0).then_inc(p_mix, 1)
                    dve.sem_inc(p_x_free, 1)
                    with dve.Fori(0, ROUNDS) as i:
                        one_hots(i, 0)
                        dve.wait_ge(p_qe, i + 1)
                        dve.scalar_tensor_tensor(out=q_phi[:, :, :], in0=q_e[:, :, :], scalar=1.0,
                                                 in1=q_r[:, :, :], op0=ALU.min, op1=ALU.add).then_inc(p_q, 1)
                        one_hots(i, 1)
                        dve.wait_ge(p_num, i + 1)
                        for u in range(2):
                            num = bank[4 + u][0:R, 0:264].rearrange("p (h d) -> p h d", h=2)
                            dve.tensor_scalar(den[:, u, :, :], num[:, :, 128:132], 1e-6, None, ALU.add)
                        dve.drain()
                        dve.reciprocal(zed[:, :, :, :], den[:, :, :, :])
                        dve.drain()
                        for u in range(2):
                            num = bank[4 + u][0:R, 0:264].rearrange("p (h d) -> p h d", h=2)
                            for h in range(2):
                                last = dve.tensor_tensor(
                                    att[:, u, h * 128:(h + 1) * 128].rearrange("p (a d) -> p a d", a=4),
                                    num[:, h, 0:128].rearrange("p (a d) -> p a d", a=4),
                                    zed[:, u, h, :].unsqueeze(2).broadcast_to([R, 4, DH]), ALU.mult)
                        last.then_inc(p_att, 1)
                        dve.wait_ge(p_x, i * 16 + 16)
                        dve.wait_ge(p_proj, i + 1)
                        dve.tensor_tensor(res[:, :, :], bank[6][0:R, :].rearrange("p (u d) -> p u d", u=2),
                                          xn_p[:, :, :], ALU.add)
                        dve.drain().then_inc(p_x_free, 1)
                        dve.tensor_tensor(res[:, :, :], res[:, :, :], both(row_bias["bo"]), ALU.add)
                        dve.drain()
                        ln_stats(dve, res, stats, mv, p_var)
                        dve.wait_ge(p_root, i * 2 + 1)
                        ln_scale(dve, x1, res, mv, std, rstd)
                        dve.drain()
                        dve.tensor_tensor(x1[:, :, :], x1[:, :, :], both(row_bias["ln1_g"]), ALU.mult)
                        dve.drain()
                        dve.tensor_tensor(x1[:, :, :], x1[:, :, :], both(row_bias["ln1_b"]), ALU.add) \
                            .then_inc(p_x1, 1)
                        one_hots(i, 2)
                        one_hots(i, 3)
                        dve.wait_ge(p_f2, i + 1)
                        dve.tensor_tensor(res[:, :, :], bank[3][0:R, :].rearrange("p (u d) -> p u d", u=2),
                                          x1[:, :, :], ALU.add)
                        dve.drain()
                        dve.tensor_tensor(res[:, :, :], res[:, :, :], both(row_bias["b2"]), ALU.add)
                        dve.drain()
                        ln_stats(dve, res, stats, mv, p_var)
                        dve.wait_ge(p_root, i * 2 + 2)
                        dve.wait_ge(p_stored, i * 16 + 16)
                        ln_scale(dve, mix, res, mv, std, rstd)
                        dve.drain()
                        dve.tensor_tensor(mix[:, :, :], mix[:, :, :], both(row_bias["ln2_g"]), ALU.mult)
                        dve.drain()
                        dve.tensor_tensor(mix[:, :, :], mix[:, :, :], both(row_bias["ln2_b"]), ALU.add) \
                            .then_inc(p_mix, 1)

                @block.scalar
                def _(act):
                    def keep_sums(i, q):
                        first, last, shift = steps(act, i * SLOTS + q)
                        with act.Fori(first, last) as n:
                            tile = tile_of(act, n, shift)
                            act.wait_ge(sums_made, n + 1)
                            act.copy(acc[:, bass.ds(tile * D, D)], sums[0:R, bass.ds((n % 2) * 512, D)]) \
                                .then_inc(sums_kept, 1)

                    def keep_transposed(to, there, signal, i):
                        act.wait_ge(there, i + 1)
                        act.copy(to[:, :, :], bank[2][:, 0:4 * R].rearrange("p (k n) -> p k n", k=KD)) \
                            .then_inc(signal, 1)

                    with act.Fori(0, ROUNDS) as i:
                        keep_sums(i, 0)
                        keep_transposed(xT, p_xT_ps, p_xT, i)
                        act.wait_ge(p_q_ps, i + 1)
                        for f, to in ((ACT.Exp, q_e), (ACT.Relu, q_r)):
                            for m in range(KD):
                                last = act.activation(to[:, m, :], bank[3][:, m * 2 * R:(m + 1) * 2 * R], f,
                                                      bias=col_bq[:, m:m + 1])
                        last.then_inc(p_qe, 1)
                        keep_sums(i, 1)
                        keep_transposed(attT, p_attT_ps, p_attT, i)
                        act.wait_ge(p_var, i * 2 + 1)
                        ln_root(act, mv, std, p_root)
                        keep_sums(i, 2)
                        keep_transposed(xT, p_x1T_ps, p_x1T, i)
                        for c in range(FC):
                            if c % 2 == 0:
                                act.wait_ge(p_f1, i * (FC // 2) + c // 2 + 1)
                            last = act.activation(ff[:, c, :],
                                                  bank[4 + c // 2][:, (c % 2) * 2 * R:(c % 2 + 1) * 2 * R],
                                                  ACT.Relu, bias=col_b1[:, c:c + 1])
                        last.then_inc(p_ff, 1)
                        keep_sums(i, 3)
                        act.wait_ge(p_var, i * 2 + 2)
                        ln_root(act, mv, std, p_root)

                @block.tensor
                def _(pe):
                    def sum_edges(i, q):
                        first, last, shift = steps(pe, i * SLOTS + q)
                        pe.wait_ge(gathered[q], i * (16 * GT) + 16 * GT)
                        pe.sem_inc(passed_pe, 1)
                        with pe.Fori(first, last) as n:
                            tile = tile_of(pe, n, shift)
                            half = pe.snap(n % 2)
                            to = sums[0:R, bass.ds(half * 512, D)]
                            pe.wait_ge(hot_made, n + 1)
                            for j in range(GT):
                                w = one_hot[:, bass.ds(half, 1), :, j:j + 1].squeeze(1).squeeze(2)
                                pe.matmul(to, w, ring[:, q, j, 0:D], start=(j == 0), stop=False)
                                pe.matmul(to, w, ring[:, q, j, D:2 * D], start=False, stop=False)
                            pe.wait_ge(sums_kept, n)
                            pe.matmul(to, ident[0:R, 0:R], acc[:, bass.ds(tile * D, D)], start=False, stop=True) \
                                .then_inc(sums_made, 1)
                            pe.sem_inc(hot_used, 1)
                        pe.drain().then_inc(ring_read[q], 1)

                    def transposes(rows):
                        for k in range(KD):
                            for u in range(2):
                                last = pe.transpose(bank[2][:, (2 * k + u) * R:(2 * k + u + 1) * R],
                                                    rows[:, u, k * 128:(k + 1) * 128], ident[0:R, 0:R])
                        return last

                    pe.wait_ge(w1_there, 16)
                    pe.wait_ge(w2_there, 16)
                    with pe.Fori(0, ROUNDS) as i:
                        sum_edges(i, 0)
                        pe.wait_ge(p_x, i * 16 + 16)
                        transposes(xn_p).then_inc(p_xT_ps, 1)
                        pe.wait_ge(p_xT, i + 1)
                        for m in range(KD):
                            for k in range(KD):
                                last = pe.matmul(bank[3][:, m * 2 * R:(m + 1) * 2 * R],
                                                 w_q[:, k, m * 128:(m + 1) * 128], xT[:, k, :],
                                                 start=(k == 0), stop=(k == KD - 1))
                        last.then_inc(p_q_ps, 1)
                        sum_edges(i, 1)
                        pe.wait_ge(p_q, i + 1)
                        for u in range(2):
                            for h in range(2):
                                last = pe.matmul(bank[4 + u][0:R, h * 132:(h + 1) * 132],
                                                 q_phi[:, h, u * R:(u + 1) * R], kvbd[:, h, :],
                                                 start=True, stop=True)
                        last.then_inc(p_num, 1)
                        pe.wait_ge(p_att, i + 1)
                        transposes(att).then_inc(p_attT_ps, 1)
                        pe.wait_ge(p_attT, i + 1)
                        for u in range(2):
                            for k in range(KD):
                                last = pe.matmul(bank[6][0:R, u * D:(u + 1) * D], attT[:, k, u * R:(u + 1) * R],
                                                 w_o[:, k, :], start=(k == 0), stop=(k == KD - 1))
                        last.then_inc(p_proj, 1)
                        sum_edges(i, 2)
                        pe.wait_ge(p_x1, i + 1)
                        transposes(x1).then_inc(p_x1T_ps, 1)
                        pe.wait_ge(p_x1T, i + 1)
                        for c in range(FC):
                            for k in range(KD):
                                last = pe.matmul(bank[4 + c // 2][:, (c % 2) * 2 * R:(c % 2 + 1) * 2 * R],
                                                 w_1[:, k, c * 128:(c + 1) * 128], xT[:, k, :],
                                                 start=(k == 0), stop=(k == KD - 1))
                            if c % 2:
                                last.then_inc(p_f1, 1)
                        sum_edges(i, 3)
                        pe.wait_ge(p_ff, i + 1)
                        for u in range(2):
                            for c in range(FC):
                                last = pe.matmul(bank[3][0:R, u * D:(u + 1) * D], ff[:, c, u * R:(u + 1) * R],
                                                 w_2[:, c, :], start=(c == 0), stop=(c == FC - 1))
                        last.then_inc(p_f2, 1)

        with ExitStack() as s:
            def tb(name, shape, dt=F32):
                return s.enter_context(nc.sbuf_tensor(name, shape, dt))

            x_f = tb("x_f", [R, 2, 2, D])
            mix_f = tb("mix_f", [R, 2, 2, D])
            agg = tb("agg", [R, 2, D])
            aggT = tb("aggT", [128, KD, 2 * R])
            gcn = tb("gcn", [R, 2, D])
            x2 = tb("x2", [R, 2, D])
            xt = tb("xt", [R, 2, D])
            xtT = tb("xtT", [128, KD, 2 * R])
            stats = tb("f_stats", [R, 2, 6])
            mv = tb("f_mv", [R, 2, 2])
            std = tb("f_std", [R, 2])
            rstd = tb("f_rstd", [R, 2])
            (f_in, f_free, f_agg, f_aggT_ps, f_aggT, f_gcn, f_var, f_root, f_x2, f_stored, f_xt, f_xtT_ps, f_xtT,
             f_lg) = (sem("f_" + n) for n in ("in", "free", "agg", "aggT_ps", "aggT", "gcn", "var", "root", "x2",
                                              "stored", "xt", "xtT_ps", "xtT", "lg"))
            x_v, mix_v, x2_v = pairs(a["x"]), pairs(mix_d), pairs(x2_d)

            with nc.Block() as block:
                @block.sync
                def _(sp):
                    with sp.Fori(0, PAIRS) as i:
                        sp.wait_ge(f_in, i * 32)
                        sp.sem_inc(passed_sp, 1)
                        sp.wait_ge(f_free, i + 1)
                        sp.sem_inc(passed_sp, 1)
                        sp.dma_start(x_f[:, bass.ds(i % 2, 1), :, :].squeeze(1), x_v[i]).then_inc(f_in, 16)
                        sp.dma_start(mix_f[:, bass.ds(i % 2, 1), :, :].squeeze(1), mix_v[i + 1]).then_inc(f_in, 16)
                    sp.wait_ge(f_in, 32 * PAIRS)

                @block.gpsimd
                def _(pool):
                    with pool.Fori(0, PAIRS) as i:
                        pool.wait_ge(f_x2, i + 1)
                        pool.sem_inc(passed_pool, 1)
                        pool.dma_start(x2_v[i], x2[:, :, :]).then_inc(f_stored, 16)
                    pool.wait_ge(f_stored, 16 * PAIRS)

                @block.vector
                def _(dve):
                    dve.sem_inc(f_free, 2)
                    with dve.Fori(0, PAIRS) as i:
                        own = acc[:, bass.ds(i * (2 * D), 2 * D)].rearrange("p (u d) -> p u d", u=2)
                        for u in range(2):
                            last = dve.tensor_scalar(agg[:, u, :], acc[:, bass.ds((i * 2 + u) * D, D)],
                                                     dinv_down[:, bass.ds(i * 2 + u, 1)], None, ALU.mult)
                        last.then_inc(f_agg, 1)
                        dve.wait_ge(f_gcn, i + 1)
                        dve.tensor_tensor(gcn[:, :, :], bank[3][0:R, :].rearrange("p (u d) -> p u d", u=2),
                                          both(row_bias["gnn_b"]), ALU.add)
                        dve.drain()
                        ln_stats(dve, gcn, stats, mv, f_var)
                        dve.wait_ge(f_root, i * 3 + 1)
                        ln_scale(dve, gcn, gcn, mv, std, rstd)
                        dve.drain()
                        dve.tensor_tensor(gcn[:, :, :], gcn[:, :, :], both(row_bias["gnn_gamma"]), ALU.mult)
                        dve.drain()
                        dve.tensor_tensor(gcn[:, :, :], gcn[:, :, :], both(row_bias["gnn_beta"]), ALU.add)
                        dve.drain()
                        dve.wait_ge(f_in, i * 32 + 32)
                        dve.scalar_tensor_tensor(out=gcn[:, :, :], in0=gcn[:, :, :], scalar=0.0,
                                                 in1=x_f[:, bass.ds(i % 2, 1), :, :].squeeze(1),
                                                 op0=ALU.max, op1=ALU.add)
                        dve.drain()
                        dve.wait_ge(f_stored, i * 16)
                        dve.tensor_tensor(x2[:, :, :], gcn[:, :, :], mix_f[:, bass.ds(i % 2, 1), :, :].squeeze(1),
                                          ALU.add).then_inc(f_x2, 1)
                        dve.drain().then_inc(f_free, 1)
                        ln_stats(dve, x2, stats, mv, f_var)
                        dve.wait_ge(f_root, i * 3 + 2)
                        ln_scale(dve, xt, x2, mv, std, rstd).then_inc(f_xt, 1)
                        dve.drain()
                        ln_stats(dve, xt, stats, mv, f_var)
                        dve.wait_ge(f_root, i * 3 + 3)
                        ln_scale(dve, own, xt, mv, std, rstd)
                        dve.wait_ge(f_lg, i + 1)
                        dve.tensor_tensor(logits[:, bass.ds(i * 2, 2), :],
                                          bank[5][0:R, 0:2 * EXP].rearrange("p (u e) -> p u e", u=2),
                                          row_br[0:R, :].unsqueeze(1).broadcast_to([R, 2, EXP]), ALU.add)
                        dve.drain()

                @block.scalar
                def _(act):
                    with act.Fori(0, PAIRS) as i:
                        act.wait_ge(f_aggT_ps, i + 1)
                        act.copy(aggT[:, :, :], bank[2][:, 0:4 * R].rearrange("p (k n) -> p k n", k=KD)) \
                            .then_inc(f_aggT, 1)
                        act.wait_ge(f_var, i * 3 + 1)
                        ln_root(act, mv, std, f_root)
                        act.wait_ge(f_var, i * 3 + 2)
                        ln_root(act, mv, std, f_root)
                        act.wait_ge(f_xtT_ps, i + 1)
                        act.copy(xtT[:, :, :], bank[4][:, 0:4 * R].rearrange("p (k n) -> p k n", k=KD)) \
                            .then_inc(f_xtT, 1)
                        act.wait_ge(f_var, i * 3 + 3)
                        ln_root(act, mv, std, f_root)

                @block.tensor
                def _(pe):
                    def transposes(to, rows):
                        for k in range(KD):
                            for u in range(2):
                                last = pe.transpose(to[:, (2 * k + u) * R:(2 * k + u + 1) * R],
                                                    rows[:, u, k * 128:(k + 1) * 128], ident[0:R, 0:R])
                        return last

                    with pe.Fori(0, PAIRS) as i:
                        pe.wait_ge(f_agg, i + 1)
                        transposes(bank[2], agg).then_inc(f_aggT_ps, 1)
                        pe.wait_ge(f_aggT, i + 1)
                        for u in range(2):
                            for k in range(KD):
                                last = pe.matmul(bank[3][0:R, u * D:(u + 1) * D], aggT[:, k, u * R:(u + 1) * R],
                                                 w_gt[:, k, :], start=(k == 0), stop=(k == KD - 1))
                        last.then_inc(f_gcn, 1)
                        pe.wait_ge(f_xt, i + 1)
                        transposes(bank[4], xt).then_inc(f_xtT_ps, 1)
                        pe.wait_ge(f_xtT, i + 1)
                        for u in range(2):
                            for k in range(KD):
                                last = pe.matmul(bank[5][0:R, u * EXP:(u + 1) * EXP], xtT[:, k, u * R:(u + 1) * R],
                                                 w_r[:, k, :], start=(k == 0), stop=(k == KD - 1))
                        last.then_inc(f_lg, 1)

        with ExitStack() as s:
            def tb(name, shape, dt=F32):
                return s.enter_context(nc.sbuf_tensor(name, shape, dt))

            best = tb("best", [R, 2, TILES])
            same = tb("same", [R, TILES, EXP])
            score = tb("score", [R, TILES])
            is_k = [tb(f"is_{k}", [R, TILES, EXP]) for k in range(2)]
            rest = tb("rest", [R, TILES, EXP])
            taken = tb("taken", [R, TILES, EXP])
            total = tb("total", [R, EXP, TILES])
            upto = tb("upto", [R, EXP, TILES])
            etiles = tb("etiles", [R, EXP])
            last_tile = tb("last_tile", [R, EXP])
            first_slot = tb("first_slot", [R, EXP])
            spot = tb("spot", [R, TILES, EXP])
            spot_k = tb("spot_k", [R, TILES, EXP])
            place_f = tb("place_f", [R, 2, TILES])
            past = tb("past", [1, ETILES + 1, EXP])
            expert_f = tb("expert_f", [1, ETILES + 1])
            gap = tb("gap", [R, TILES])
            ratio = tb("ratio", [R, TILES])
            one_more = tb("one_more", [R, TILES])
            r_taken, r_counts, r_gap, r_ratio = sem("r_taken"), sem("r_counts"), sem("r_gap"), sem("r_ratio")

            def over_e(v):
                return v.unsqueeze(2).broadcast_to([R, TILES, EXP])

            def over_t(v):
                return v.unsqueeze(1).broadcast_to([R, TILES, EXP])

            with nc.Block() as block:
                @block.vector
                def _(dve):
                    left = logits
                    for k in range(2):
                        dve.tensor_reduce(best[:, k, :], left[:, :, :], AX.X, ALU.max)
                        dve.drain()
                        dve.tensor_tensor(same[:, :, :], left[:, :, :], over_e(best[:, k, :]), ALU.is_equal)
                        dve.drain()
                        dve.tensor_tensor(same[:, :, :], same[:, :, :], over_t(rank[:, :]), ALU.mult)
                        dve.drain()
                        dve.tensor_reduce(score[:, :], same[:, :, :], AX.X, ALU.max)
                        dve.drain()
                        dve.tensor_tensor(is_k[k][:, :, :], over_t(rank[:, :]), over_e(score[:, :]), ALU.is_equal)
                        dve.drain()
                        if k == 0:
                            dve.scalar_tensor_tensor(out=rest[:, :, :], in0=is_k[0][:, :, :], scalar=LOWEST,
                                                     in1=logits[:, :, :], op0=ALU.mult, op1=ALU.add)
                            dve.drain()
                            left = rest
                    dve.tensor_tensor(taken[:, :, :], is_k[0][:, :, :], is_k[1][:, :, :], ALU.add) \
                        .then_inc(r_taken, 1)
                    dve.tensor_tensor(gap[:, :], best[:, 1, :], best[:, 0, :], ALU.subtract).then_inc(r_gap, 1)
                    dve.wait_ge(r_ratio, 1)
                    dve.tensor_scalar(one_more[:, :], ratio[:, :], 1.0, None, ALU.add)
                    dve.drain()
                    dve.reciprocal(weights[:, :, 0], one_more[:, :])
                    dve.drain()
                    dve.tensor_tensor(weights[:, :, 1], ratio[:, :], weights[:, :, 0], ALU.mult)
                    dve.wait_ge(r_counts, 1)
                    dve.tensor_copy(total[:, :, :], bank[3][0:R, 0:TILES * EXP].rearrange("p (t e) -> p e t", e=EXP))
                    dve.drain()
                    for e in range(EXP):
                        dve.tensor_tensor_scan(upto[:, e, :], ones[0:R, 0:TILES], total[:, e, :], 0.0,
                                               ALU.mult, ALU.add)
                    dve.drain()
                    dve.tensor_scalar(etiles[:, :], upto[:, :, TILES - 1], (ET - 1) / 2.0, 1.0 / ET, ALU.add, ALU.mult)
                    dve.drain()
                    dve.tensor_tensor(upto[:, :, :], upto[:, :, :], total[:, :, :], ALU.subtract)
                    dve.drain()
                    dve.tensor_scalar(etiles[:, :], etiles[:, :], ROUND, -ROUND, ALU.add, ALU.add)
                    dve.drain()
                    dve.tensor_tensor_scan(last_tile[:, :], ones[0:R, 0:EXP], etiles[:, :], 0.0, ALU.mult, ALU.add)
                    dve.drain()
                    dve.tensor_tensor(first_slot[:, :], last_tile[:, :], etiles[:, :], ALU.subtract)
                    dve.drain()
                    dve.tensor_scalar(first_slot[:, :], first_slot[:, :], float(ET), None, ALU.mult)
                    dve.tensor_tensor(spot[:, :, :], bank[2][0:R, 0:TILES * EXP].rearrange("p (t e) -> p t e", e=EXP),
                                      upto[:, :, :].rearrange("p e t -> p t e"), ALU.add)
                    dve.drain()
                    dve.tensor_tensor(spot[:, :, :], spot[:, :, :], over_t(first_slot[:, :]), ALU.add)
                    dve.drain()
                    for k in range(2):
                        dve.tensor_tensor(spot_k[:, :, :], spot[:, :, :], is_k[k][:, :, :], ALU.mult)
                        dve.drain()
                        dve.tensor_reduce(place_f[:, k, :], spot_k[:, :, :], AX.X, ALU.add)
                        dve.drain()
                        dve.tensor_copy(place[:, :, k], place_f[:, k, :])
                    dve.tensor_tensor(past[:, :, :], tile_no[:, :].unsqueeze(2).broadcast_to([1, ETILES + 1, EXP]),
                                      last_tile[0:1, :].unsqueeze(1).broadcast_to([1, ETILES + 1, EXP]), ALU.is_ge)
                    dve.drain()
                    dve.tensor_reduce(expert_f[:, :], past[:, :, :], AX.X, ALU.add)
                    dve.drain()
                    dve.tensor_scalar(expert_of[:, :], expert_f[:, :], float(EXP - 1), None, ALU.min)

                @block.scalar
                def _(act):
                    act.wait_ge(r_gap, 1)
                    act.activation(ratio[:, :], gap[:, :], ACT.Exp).then_inc(r_ratio, 1)

                @block.tensor
                def _(pe):
                    pe.wait_ge(r_taken, 1)
                    flat = taken[:, :, :].rearrange("p t e -> p (t e)")
                    pe.matmul(bank[2][0:R, 0:TILES * EXP], before[:, :], flat, start=True, stop=True)
                    pe.matmul(bank[3][0:R, 0:TILES * EXP], ones[0:R, 0:R], flat, start=True, stop=True) \
                        .then_inc(r_counts, 1)

        BUFS = 5
        with ExitStack() as s:
            rows = s.enter_context(nc.sbuf_tensor("rows", [R, BUFS, 2, D], F32))
            spots = s.enter_context(nc.sbuf_tensor("spots", [R, BUFS, 4], I32))
            s_rows = [sem(f"s_rows{k}") for k in range(BUFS)]
            s_out = [sem(f"s_out{k}") for k in range(BUFS)]
            with nc.Block() as block:
                @block.vector
                def _(dve):
                    with dve.Fori(0, PAIRS // BUFS) as i:
                        for k in range(BUFS):
                            dve.wait_ge(s_out[k], i * 64)
                            dve.tensor_copy(rows[:, k, :, :].rearrange("p u d -> p (u d)"),
                                            acc[:, bass.ds((i * BUFS + k) * 2 * D, 2 * D)])
                            dve.tensor_copy(spots[:, k, :].rearrange("p (u c) -> p u c", u=2),
                                            place[:, bass.ds((i * BUFS + k) * 2, 2), :])
                            dve.drain().then_inc(s_rows[k], 1)

                @block.gpsimd
                def _(pool):
                    with pool.Fori(0, PAIRS // BUFS) as i:
                        for k in range(BUFS):
                            pool.wait_ge(s_rows[k], i + 1)
                            pool.sem_inc(passed_pool, 1)
                            for u in range(2):
                                for c in range(2):
                                    pool.indirect_dma_start(
                                        slot_d, bass.IndirectOffsetOnAxis(spots[:, k, 2 * u + c:2 * u + c + 1], 0),
                                        rows[:, k, u, :], None).then_inc(s_out[k], 16)
                    for k in range(BUFS):
                        pool.wait_ge(s_out[k], 64 * (PAIRS // BUFS))

        with ExitStack() as s:
            def tb(name, shape, dt=F32):
                return s.enter_context(nc.sbuf_tensor(name, shape, dt))

            e_w1 = [tb(f"e_w1{b}", [128, KD, FF]) for b in range(2)]
            e_w2 = [tb(f"e_w2{b}", [128, FC, D]) for b in range(2)]
            e_g = [tb(f"e_g{b}", [128, KD]) for b in range(2)]
            e_b = [tb(f"e_b{b}", [128, KD]) for b in range(2)]
            e_b1 = [tb(f"e_b1{b}", [128, FC]) for b in range(2)]
            e_b2 = [tb(f"e_b2{b}", [128, D]) for b in range(2)]
            e_x = [tb(f"e_x{b}", [128, 2, D]) for b in range(2)]
            e_xT = [tb(f"e_xT{b}", [128, KD, ET]) for b in range(2)]
            e_h = tb("e_h", [128, FC, ET])
            e_y = [tb(f"e_y{b}", [128, 2, D]) for b in range(2)]
            w_in = [sem(f"w_in{b}") for b in range(2)]
            b2_in = [sem(f"b2_in{b}") for b in range(2)]
            x_in_e = [sem(f"x_in_e{b}") for b in range(2)]
            t_ps, t_on, l1_ps, l1_on, l2_ps, y_made = (sem("e_" + n) for n in ("t_ps", "t_on", "l1_ps", "l1_on",
                                                                                "l2_ps", "y_made"))
            y_out = [sem(f"y_out{b}") for b in range(2)]
            slot_v = slot_d.rearrange("(n u p) d -> n p u d", u=2, p=128)
            y_v = y_d.rearrange("(n u p) d -> n p u d", u=2, p=128)
            TURNS = ETILES // 2

            with nc.Block() as block:
                @block.sync
                def _(sp):
                    def load(tile, b, gate):
                        e = sp.value_load(expert_of[0:1, bass.ds(tile, 1)], min_val=0, max_val=EXP - 1)
                        if gate:
                            sp.wait_ge(y_made, tile - 1)
                            sp.sem_inc(passed_sp, 1)
                        sp.dma_start(e_x[b][:, :, :], slot_v[tile]).then_inc(x_in_e[b], 16)
                        sp.dma_start(e_g[b][:, :], a["e_g"][e]).then_inc(x_in_e[b], 16)
                        sp.dma_start(e_b[b][:, :], a["e_b"][e]).then_inc(x_in_e[b], 16)
                        sp.dma_start(e_w1[b][:, :, :], a["e_W1"][e].rearrange("(k p) n -> p k n", p=128)) \
                            .then_inc(w_in[b], 16)
                        sp.dma_start(e_b1[b][:, :], a["e_b1"][e]).then_inc(w_in[b], 16)
                        sp.dma_start(e_w2[b][:, :, :], a["e_W2"][e].rearrange("(k p) n -> p k n", p=128)) \
                            .then_inc(w_in[b], 16)
                        sp.dma_start(e_b2[b][:, :], a["e_b2"][e].partition_broadcast(128)).then_inc(b2_in[b], 16)

                    load(0, 0, False)
                    load(1, 1, False)
                    with sp.Fori(1, TURNS) as i:
                        load(i * 2, 0, True)
                        load(i * 2 + 1, 1, True)
                    sp.wait_ge(y_made, ETILES - 1)
                    sp.dma_start(e_x[0][:, :, :], slot_v[ETILES]).then_inc(x_in_e[0], 48)
                    for b in range(2):
                        sp.wait_ge(x_in_e[b], 48 * (TURNS + 1 - b))

                @block.gpsimd
                def _(pool):
                    with pool.Fori(0, TURNS) as i:
                        for b in range(2):
                            pool.wait_ge(y_made, i * 2 + b + 1)
                            pool.sem_inc(passed_pool, 1)
                            pool.dma_start(y_v[i * 2 + b], e_y[b][:, :, :]).then_inc(y_out[b], 16)
                    for b in range(2):
                        pool.wait_ge(y_out[b], 16 * TURNS)

                @block.vector
                def _(dve):
                    def scaled(tile, b):
                        dve.wait_ge(t_ps, tile + 1)
                        for k in range(KD):
                            last = dve.tensor_scalar(e_xT[b][:, k, :], bank[b][:, k * ET:(k + 1) * ET],
                                                     e_g[b][:, k:k + 1], e_b[b][:, k:k + 1], ALU.mult, ALU.add)
                        last.then_inc(t_on, 1)

                    scaled(0, 0)
                    with dve.Fori(0, TURNS) as i:
                        for b in range(2):
                            tile = i * 2 + b
                            scaled(tile + 1, 1 - b)
                            dve.wait_ge(l2_ps, tile + 1)
                            dve.wait_ge(y_out[b], i * 16)
                            dve.wait_ge(b2_in[b], i * 16 + 16)
                            dve.tensor_tensor(e_y[b][:, :, :], bank[2 + b][:, :].rearrange("p (u d) -> p u d", u=2),
                                              e_b2[b][:, :].unsqueeze(1).broadcast_to([128, 2, D]), ALU.add) \
                                .then_inc(y_made, 1)

                @block.scalar
                def _(act):
                    with act.Fori(0, TURNS) as i:
                        for b in range(2):
                            tile = i * 2 + b
                            act.wait_ge(l2_ps, tile)
                            for c in range(FC):
                                if c % 2 == 0:
                                    act.wait_ge(l1_ps, tile * (FC // 2) + c // 2 + 1)
                                last = act.activation(e_h[:, c, :], bank[4 + c // 2][:, (c % 2) * ET:(c % 2 + 1) * ET],
                                                      ACT.Gelu, bias=e_b1[b][:, c:c + 1])
                                if c % 2:
                                    last.then_inc(l1_on, 1)

                @block.tensor
                def _(pe):
                    def turned(tile, b, turn):
                        pe.wait_ge(x_in_e[b], turn * 48 + 48)
                        for k in range(KD):
                            for u in range(2):
                                last = pe.transpose(bank[b][:, k * ET + u * 128:k * ET + (u + 1) * 128],
                                                    e_x[b][:, u, k * 128:(k + 1) * 128], ident[:, :])
                        last.then_inc(t_ps, 1)

                    turned(0, 0, 0)
                    with pe.Fori(0, TURNS) as i:
                        for b in range(2):
                            tile = i * 2 + b
                            pe.wait_ge(w_in[b], i * 48 + 48)
                            pe.wait_ge(t_on, tile + 1)
                            for c in range(FC):
                                for k in range(KD):
                                    last = pe.matmul(bank[4 + c // 2][:, (c % 2) * ET:(c % 2 + 1) * ET],
                                                     e_w1[b][:, k, c * 128:(c + 1) * 128], e_xT[b][:, k, :],
                                                     start=(k == 0), stop=(k == KD - 1))
                                if c % 2:
                                    last.then_inc(l1_ps, 1)
                            turned(tile + 1, 1 - b, i + b)
                            for u in range(2):
                                for c in range(FC):
                                    if u == 0 and c % 2 == 0:
                                        pe.wait_ge(l1_on, tile * (FC // 2) + c // 2 + 1)
                                    last = pe.matmul(bank[2 + b][:, u * D:(u + 1) * D],
                                                     e_h[:, c, u * 128:(u + 1) * 128], e_w2[b][:, c, :],
                                                     start=(c == 0), stop=(c == FC - 1))
                            last.then_inc(l2_ps, 1)

        with ExitStack() as s:
            got = s.enter_context(nc.sbuf_tensor("got", [R, BUFS, 4, D], F32))
            spots = s.enter_context(nc.sbuf_tensor("spots_c", [R, BUFS, 4], I32))
            x2_c = s.enter_context(nc.sbuf_tensor("x2_c", [R, BUFS, 2, D], F32))
            half = s.enter_context(nc.sbuf_tensor("half", [R, BUFS, 2, D], F32))
            res = s.enter_context(nc.sbuf_tensor("res_c", [R, BUFS, 2, D], F32))
            c_spots = [sem(f"c_spots{k}") for k in range(BUFS)]
            c_got = [sem(f"c_got{k}") for k in range(BUFS)]
            c_x2 = [sem(f"c_x2{k}") for k in range(BUFS)]
            c_res = [sem(f"c_res{k}") for k in range(BUFS)]
            c_out = [sem(f"c_out{k}") for k in range(BUFS)]
            x2_v, out_v = pairs(x2_d), pairs(out)
            with nc.Block() as block:
                @block.sync
                def _(sp):
                    with sp.Fori(0, PAIRS // BUFS) as i:
                        for k in range(BUFS):
                            sp.wait_ge(c_res[k], i)
                            sp.sem_inc(passed_sp, 1)
                            sp.dma_start(x2_c[:, k, :, :], x2_v[i * BUFS + k]).then_inc(c_x2[k], 16)
                    for k in range(BUFS):
                        sp.wait_ge(c_x2[k], 16 * (PAIRS // BUFS))

                @block.gpsimd
                def _(pool):
                    with pool.Fori(0, PAIRS // BUFS) as i:
                        for k in range(BUFS):
                            pool.wait_ge(c_spots[k], i + 1)
                            pool.sem_inc(passed_pool, 1)
                            for c in range(4):
                                pool.indirect_dma_start(got[:, k, c, :], None, y_d,
                                                        bass.IndirectOffsetOnAxis(spots[:, k, c:c + 1], 0)) \
                                    .then_inc(c_got[k], 16)

                @block.vector
                def _(dve):
                    def set_spots(pair, k):
                        dve.tensor_copy(spots[:, k, :].rearrange("p (u c) -> p u c", u=2), place[:, pair, :]) \
                            .then_inc(c_spots[k], 1)

                    for k in range(BUFS):
                        set_spots(slice(2 * k, 2 * k + 2), k)
                    with dve.Fori(0, PAIRS // BUFS) as i:
                        for k in range(BUFS):
                            dve.wait_ge(c_x2[k], i * 16 + 16)
                            dve.wait_ge(c_got[k], i * 64 + 64)
                            dve.wait_ge(c_out[k], i * 16)
                            for u in range(2):
                                dve.scalar_tensor_tensor(
                                    out=half[:, k, u, :], in0=got[:, k, 2 * u, :],
                                    scalar=weights[:, bass.ds((i * BUFS + k) * 2 + u, 1), 0],
                                    in1=x2_c[:, k, u, :], op0=ALU.mult, op1=ALU.add)
                            dve.drain()
                            for u in range(2):
                                last = dve.scalar_tensor_tensor(
                                    out=res[:, k, u, :], in0=got[:, k, 2 * u + 1, :],
                                    scalar=weights[:, bass.ds((i * BUFS + k) * 2 + u, 1), 1],
                                    in1=half[:, k, u, :], op0=ALU.mult, op1=ALU.add)
                            last.then_inc(c_res[k], 1)
                            dve.drain()
                            nxt = nc.s_assert_within(
                                dve.snap(((i * BUFS + k) * 2 + 2 * BUFS) % (2 * PAIRS)), 0, TILES - 2,
                                skip_runtime_bounds_check_because="it is even and a remainder of TILES")
                            set_spots(bass.ds(nxt, 2), k)

                @block.scalar
                def _(act):
                    with act.Fori(0, PAIRS // BUFS) as i:
                        for k in range(BUFS):
                            act.wait_ge(c_res[k], i + 1)
                            act.dma_start(out_v[i * BUFS + k], res[:, k, :, :]).then_inc(c_out[k], 16)
                    for k in range(BUFS):
                        act.wait_ge(c_out[k], 16 * (PAIRS // BUFS))


_NAMES = {
    "x": "x", "src": "src", "dst": "dst", "gnn_W": "L0_gnn_W", "gnn_b": "L0_gnn_b",
    "gnn_gamma": "L0_gnn_gamma", "gnn_beta": "L0_gnn_beta", "Wq": "L0_mix_Wq", "bq": "L0_mix_bq",
    "Wk": "L0_mix_Wk", "bk": "L0_mix_bk", "Wv": "L0_mix_Wv", "bv": "L0_mix_bv", "Wo": "L0_mix_Wo",
    "bo": "L0_mix_bo", "W1": "L0_mix_W1", "b1": "L0_mix_b1", "W2": "L0_mix_W2", "b2": "L0_mix_b2",
    "ln1_g": "L0_mix_ln1_g", "ln1_b": "L0_mix_ln1_b", "ln2_g": "L0_mix_ln2_g", "ln2_b": "L0_mix_ln2_b",
    "Wr": "L0_ffn_Wr", "br": "L0_ffn_br", "e_g": "L0_ffn_ln_g", "e_b": "L0_ffn_ln_b",
    "e_W1": "L0_ffn_W1", "e_b1": "L0_ffn_b1", "e_W2": "L0_ffn_W2", "e_b2": "L0_ffn_b2",
}


def kernel(**inputs):
    import numpy as np
    import concourse.bacc as bacc
    from concourse.bass_utils import run_bass_kernel_spmd as run

    def columns(v):
        return v.reshape(EXP, -1, 128).transpose(0, 2, 1)

    nc = bacc.Bacc("TRN2", target_bir_lowering=False, num_devices=1)
    arrays, args = {}, {}
    for short, name in _NAMES.items():
        v = np.asarray(inputs[name])
        if short in ("e_g", "e_b", "e_b1"):
            v = columns(v)
        v = np.ascontiguousarray(v)
        arrays["in_" + short] = v
        args[short] = nc.dram_tensor("in_" + short, v.shape, mybir.dt.from_np(v.dtype), kind="ExternalInput").ap()
    out = nc.dram_tensor("out", (NODES, D), F32, kind="ExternalOutput").ap()
    gps_layer(nc, args, out)
    return run(nc, [arrays], core_ids=[0]).results[0]["out"]
```
